# Optimizing a Trainium2 kernel written in Bass

```python
import numpy as np
import jax
import jax.numpy as jnp

def _softmax(x, axis=-1):
    return jax.nn.softmax(x, axis=axis)

def _gelu(x):
    return jax.nn.gelu(x, approximate=True)

def _silu(x):
    return jax.nn.silu(x)

def _sigmoid(x):
    return jax.nn.sigmoid(x)

def _layernorm(x, axis=-1, eps=1e-05):
    m = jnp.mean(x, axis=axis, keepdims=True)
    v = jnp.var(x, axis=axis, keepdims=True)
    return (x - m) / jnp.sqrt(v + eps)

def _scatter_add(tgt, idx, src, axis=0):
    return tgt.at[idx].add(src)

def _segment_sum(src, seg, n):
    return jax.ops.segment_sum(src, seg, n)
kernel_name = 'mk_macaron_d1_jaxref_r8_8fe0b8'

def setup_inputs(seed: int=0):
    np.random.seed(seed)
    _w = jnp.asarray

    def _L0_attn_setup():
        import jax, jax.numpy as jnp
        import numpy as np
        B, T, H = (2, 512, 256)
        NH, DK, DV = (16, 128, 128)
        CONV = 4
        MLP_H = 32
        EPS_STAT = 1e-06
        NORM_EPS = 1e-05
        L2_EPS = 1e-06

        def short_conv(x, w):
            K = w.shape[-1]
            xp = jnp.pad(x, ((0, 0), (K - 1, 0), (0, 0)))
            y = sum((xp[:, i:i + x.shape[1], :] * w[:, i] for i in range(K)))
            return jax.nn.silu(y)

        def _mlp(s, W1, b1, W2, b2):
            return (jax.nn.silu(s @ W1.T + b1) @ W2.T + b2)[..., 0]
        key = jax.random.key(seed)
        ks = jax.random.split(key, 20)

        def w(k, shape, scale=None):
            scale = 1.0 / np.sqrt(shape[-1]) if scale is None else scale
            return jax.random.normal(k, shape, jnp.float32) * scale
        return dict(hidden_states=jax.random.normal(ks[0], (B, T, H), jnp.float32), Wq=w(ks[1], (NH * DK, H)), Wk=w(ks[2], (NH * DK, H)), Wv=w(ks[3], (NH * DV, H)), conv_q=w(ks[4], (NH * DK, CONV), 0.5), conv_k=w(ks[5], (NH * DK, CONV), 0.5), conv_v=w(ks[6], (NH * DV, CONV), 0.5), A_log=jnp.log(jax.random.uniform(ks[7], (NH,), jnp.float32, 1.0, 16.0)), dt_bias=jnp.zeros((NH * DK,), jnp.float32), Wsv=w(ks[8], (DV, DK)), Wb1=w(ks[9], (MLP_H, 3)), bb1=jnp.zeros((MLP_H,), jnp.float32), Wb2=w(ks[10], (1, MLP_H)), bb2=jnp.zeros((1,), jnp.float32), Wa1=w(ks[11], (MLP_H, 3)), ba1=jnp.zeros((MLP_H,), jnp.float32), Wa2=w(ks[12], (1, MLP_H)), ba2=jnp.zeros((1,), jnp.float32), Wg1=w(ks[13], (DV, H)), Wg2=w(ks[14], (NH * DV, DV)), bg2=jnp.zeros((NH * DV,), jnp.float32), norm_w=jnp.ones((DV,), jnp.float32), Wo=w(ks[15], (H, NH * DV)))
    _L0_attn_in = _L0_attn_setup()

    def _L0_ffn_setup():
        import jax, jax.numpy as jnp
        import numpy as np
        H = 256
        E = 16
        K = 4
        I = 176
        IS = 176 * 2
        B, S = (1, 128)
        key = jax.random.key(seed)
        ks = jax.random.split(key, 9)
        scale = 0.02
        return {'hidden_states': jax.random.normal(ks[0], (B, S, H), dtype=jnp.float32), 'gate_w': jax.random.normal(ks[1], (E, H), dtype=jnp.float32) * scale, 'w_gate': jax.random.normal(ks[2], (E, H, I), dtype=jnp.float32) * scale, 'w_up': jax.random.normal(ks[3], (E, H, I), dtype=jnp.float32) * scale, 'w_down': jax.random.normal(ks[4], (E, I, H), dtype=jnp.float32) * scale, 'sw_gate': jax.random.normal(ks[5], (H, IS), dtype=jnp.float32) * scale, 'sw_up': jax.random.normal(ks[6], (H, IS), dtype=jnp.float32) * scale, 'sw_down': jax.random.normal(ks[7], (IS, H), dtype=jnp.float32) * scale}
    _L0_ffn_in = _L0_ffn_setup()
    _d = {'L0_attn_hidden_states': _L0_attn_in['hidden_states'], 'L0_attn_Wq': _L0_attn_in['Wq'], 'L0_attn_Wk': _L0_attn_in['Wk'], 'L0_attn_Wv': _L0_attn_in['Wv'], 'L0_attn_conv_q': _L0_attn_in['conv_q'], 'L0_attn_conv_k': _L0_attn_in['conv_k'], 'L0_attn_conv_v': _L0_attn_in['conv_v'], 'L0_attn_A_log': _L0_attn_in['A_log'], 'L0_attn_dt_bias': _L0_attn_in['dt_bias'], 'L0_attn_Wsv': _L0_attn_in['Wsv'], 'L0_attn_Wb1': _L0_attn_in['Wb1'], 'L0_attn_bb1': _L0_attn_in['bb1'], 'L0_attn_Wb2': _L0_attn_in['Wb2'], 'L0_attn_bb2': _L0_attn_in['bb2'], 'L0_attn_Wa1': _L0_attn_in['Wa1'], 'L0_attn_ba1': _L0_attn_in['ba1'], 'L0_attn_Wa2': _L0_attn_in['Wa2'], 'L0_attn_ba2': _L0_attn_in['ba2'], 'L0_attn_Wg1': _L0_attn_in['Wg1'], 'L0_attn_Wg2': _L0_attn_in['Wg2'], 'L0_attn_bg2': _L0_attn_in['bg2'], 'L0_attn_norm_w': _L0_attn_in['norm_w'], 'L0_attn_Wo': _L0_attn_in['Wo'], 'L0_ffn_gate_w': _L0_ffn_in['gate_w'], 'L0_ffn_w_gate': _L0_ffn_in['w_gate'], 'L0_ffn_w_up': _L0_ffn_in['w_up'], 'L0_ffn_w_down': _L0_ffn_in['w_down'], 'L0_ffn_sw_gate': _L0_ffn_in['sw_gate'], 'L0_ffn_sw_up': _L0_ffn_in['sw_up'], 'L0_ffn_sw_down': _L0_ffn_in['sw_down']}
    _x0 = _d['L0_attn_hidden_states']
    _d['L0_attn_hidden_states'] = jax.random.normal(jax.random.fold_in(jax.random.key(seed), 1), (2, 512, 256), dtype=_x0.dtype)
    del _x0
    return _d

def reference(L0_attn_hidden_states, L0_attn_Wq, L0_attn_Wk, L0_attn_Wv, L0_attn_conv_q, L0_attn_conv_k, L0_attn_conv_v, L0_attn_A_log, L0_attn_dt_bias, L0_attn_Wsv, L0_attn_Wb1, L0_attn_bb1, L0_attn_Wb2, L0_attn_bb2, L0_attn_Wa1, L0_attn_ba1, L0_attn_Wa2, L0_attn_ba2, L0_attn_Wg1, L0_attn_Wg2, L0_attn_bg2, L0_attn_norm_w, L0_attn_Wo, L0_ffn_gate_w, L0_ffn_w_gate, L0_ffn_w_up, L0_ffn_w_down, L0_ffn_sw_gate, L0_ffn_sw_up, L0_ffn_sw_down):

    def _L0_attn_ref(hidden_states, Wq, Wk, Wv, conv_q, conv_k, conv_v, A_log, dt_bias, Wsv, Wb1, bb1, Wb2, bb2, Wa1, ba1, Wa2, ba2, Wg1, Wg2, bg2, norm_w, Wo):
        import jax, jax.numpy as jnp
        import numpy as np
        B, T, H = (2, 512, 256)
        NH, DK, DV = (16, 128, 128)
        CONV = 4
        MLP_H = 32
        EPS_STAT = 1e-06
        NORM_EPS = 1e-05
        L2_EPS = 1e-06

        def short_conv(x, w):
            K = w.shape[-1]
            xp = jnp.pad(x, ((0, 0), (K - 1, 0), (0, 0)))
            y = sum((xp[:, i:i + x.shape[1], :] * w[:, i] for i in range(K)))
            return jax.nn.silu(y)

        def _mlp(s, W1, b1, W2, b2):
            return (jax.nn.silu(s @ W1.T + b1) @ W2.T + b2)[..., 0]
        x = hidden_states
        Bsz, Tlen, _ = x.shape
        q = short_conv(x @ Wq.T, conv_q).reshape(Bsz, Tlen, NH, DK)
        k = short_conv(x @ Wk.T, conv_k).reshape(Bsz, Tlen, NH, DK)
        v = short_conv(x @ Wv.T, conv_v).reshape(Bsz, Tlen, NH, DV)
        v_hat = jnp.einsum('bthk,vk->bthv', k, Wsv)
        e = v_hat - v
        s_l2 = jnp.sqrt(jnp.sum(e * e, -1) + EPS_STAT)
        s_l1 = jnp.sum(jnp.abs(e), -1)
        cos_den = jnp.sqrt(jnp.sum(v_hat * v_hat, -1) + EPS_STAT) * jnp.sqrt(jnp.sum(v * v, -1) + EPS_STAT) + EPS_STAT
        s_cos = 1.0 - jnp.sum(v_hat * v, -1) / cos_den
        s = jnp.stack([s_l2, s_l1, s_cos], -1)
        beta = jax.nn.sigmoid(_mlp(s, Wb1, bb1, Wb2, bb2))
        amp = _mlp(s, Wa1, ba1, Wa2, ba2)
        r = k / jnp.maximum(jnp.linalg.norm(k, axis=-1, keepdims=True), 1e-12)
        g_raw = r * amp[..., None]
        g = -jnp.exp(A_log)[None, None, :, None] * jax.nn.softplus(g_raw + dt_bias.reshape(NH, DK))
        qn = q * jax.lax.rsqrt(jnp.sum(q * q, -1, keepdims=True) + L2_EPS)
        kn = k * jax.lax.rsqrt(jnp.sum(k * k, -1, keepdims=True) + L2_EPS)
        scale = DK ** (-0.5)

        def step(S, inp):
            q_t, k_t, v_t, g_t, b_t = inp
            S = S * jnp.exp(g_t)[..., None]
            kv = jnp.einsum('bhk,bhkv->bhv', k_t, S)
            delta = (v_t - kv) * b_t[..., None]
            S = S + k_t[..., None] * delta[..., None, :]
            o_t = jnp.einsum('bhk,bhkv->bhv', q_t * scale, S)
            return (S, o_t)
        tfirst = lambda a: jnp.swapaxes(a, 0, 1)
        S0 = jnp.zeros((Bsz, NH, DK, DV), jnp.float32)
        _, o = jax.lax.scan(step, S0, (tfirst(qn), tfirst(kn), tfirst(v), tfirst(g), tfirst(beta)))
        o = jnp.swapaxes(o, 0, 1)
        gate = (x @ Wg1.T @ Wg2.T + bg2).reshape(Bsz, Tlen, NH, DV)
        o = o * jax.lax.rsqrt(jnp.mean(o * o, -1, keepdims=True) + NORM_EPS) * norm_w
        o = o * jax.nn.sigmoid(gate)
        return o.reshape(Bsz, Tlen, NH * DV) @ Wo.T

    def _L0_ffn_ref(hidden_states, gate_w, w_gate, w_up, w_down, sw_gate, sw_up, sw_down):
        import jax, jax.numpy as jnp
        import numpy as np
        H = 256
        E = 16
        K = 4
        I = 176
        IS = 176 * 2
        B, S = (1, 128)
        orig_shape = hidden_states.shape
        x = hidden_states.reshape(-1, H)
        T = x.shape[0]
        logits = jnp.einsum('th,eh->te', x, gate_w)
        scores = jax.nn.softmax(logits, axis=-1)
        topk_w, topk_idx = jax.lax.top_k(scores, K)
        topk_w = topk_w / jnp.sum(topk_w, axis=-1, keepdims=True)
        combine = jnp.zeros((T, E), dtype=x.dtype)
        combine = combine.at[jnp.arange(T)[:, None], topk_idx].add(topk_w)
        g = jnp.einsum('th,ehi->tei', x, w_gate)
        u = jnp.einsum('th,ehi->tei', x, w_up)
        a = jax.nn.silu(g) * u
        a = a * combine[:, :, None]
        y = jnp.einsum('tei,eih->th', a, w_down)
        sg = x @ sw_gate
        su = x @ sw_up
        y = y + jax.nn.silu(sg) * su @ sw_down
        return y.reshape(orig_shape)
    x = L0_attn_hidden_states
    x = x + 0.5 * _L0_ffn_ref(_layernorm(x, axis=-1), L0_ffn_gate_w, L0_ffn_w_gate, L0_ffn_w_up, L0_ffn_w_down, L0_ffn_sw_gate, L0_ffn_sw_up, L0_ffn_sw_down)
    x = x + _L0_attn_ref(_layernorm(x, axis=-1), L0_attn_Wq, L0_attn_Wk, L0_attn_Wv, L0_attn_conv_q, L0_attn_conv_k, L0_attn_conv_v, L0_attn_A_log, L0_attn_dt_bias, L0_attn_Wsv, L0_attn_Wb1, L0_attn_bb1, L0_attn_Wb2, L0_attn_bb2, L0_attn_Wa1, L0_attn_ba1, L0_attn_Wa2, L0_attn_ba2, L0_attn_Wg1, L0_attn_Wg2, L0_attn_bg2, L0_attn_norm_w, L0_attn_Wo)
    x = x + 0.5 * _L0_ffn_ref(_layernorm(x, axis=-1), L0_ffn_gate_w, L0_ffn_w_gate, L0_ffn_w_up, L0_ffn_w_down, L0_ffn_sw_gate, L0_ffn_sw_up, L0_ffn_sw_down)
    return x

_drawn_inputs = setup_inputs


def setup_inputs(seed=0):
    import zlib

    import numpy as np

    out = dict(_drawn_inputs(seed))
    spreads = {'L0_attn_dt_bias': (0.0, 0.8),
     'L0_attn_bb1': (0.0, 0.8),
     'L0_attn_ba1': (0.0, 0.8),
     'L0_attn_bg2': (0.0, 0.8),
     'L0_attn_norm_w': (1.0, 0.6)}
    factors = {'L0_attn_Wq': 8.0,
     'L0_attn_Wk': 8.0,
     'L0_attn_Wv': 8.0,
     'L0_attn_conv_q': 8.0,
     'L0_attn_conv_k': 8.0,
     'L0_attn_conv_v': 8.0,
     'L0_attn_A_log': 8.0,
     'L0_attn_Wsv': 8.0,
     'L0_attn_Wb2': 8.0,
     'L0_attn_Wa1': 8.0,
     'L0_attn_Wa2': 8.0,
     'L0_attn_Wg1': 8.0,
     'L0_attn_Wg2': 8.0,
     'L0_attn_Wo': 8.0,
     'L0_ffn_gate_w': 8.0,
     'L0_ffn_w_gate': 7.859,
     'L0_ffn_w_up': 7.808,
     'L0_ffn_w_down': 7.771,
     'L0_ffn_sw_gate': 2.889,
     'L0_ffn_sw_up': 2.851,
     'L0_ffn_sw_down': 2.852}
    for name, (base, spread) in spreads.items():
        noise = np.random.default_rng([zlib.crc32(name.encode()), seed]).standard_normal(out[name].shape)
        drawn = base * np.exp(spread * noise) if base else spread * noise
        out[name] = jnp.asarray(drawn.astype(out[name].dtype))
    for name, factor in factors.items():
        out[name] = (out[name] * factor).astype(out[name].dtype)
    return out
```

```python
from contextlib import ExitStack

import numpy as np

import concourse.bass as bass
from concourse import mybir

F32 = mybir.dt.float32
I32 = mybir.dt.int32
ALU = mybir.AluOpType
ACT = mybir.ActivationFunctionType
AX = mybir.AxisListType

P = 128
B, T, H = 2, 512, 256
NH, DK, CONV, MLP = 16, 128, 4, 32
E, TOPK, INTER = 16, 4, 176
TOK = B * T
TB = TOK // P
KB = H // P
NC = T // P
LEVELS = 7
HALF = P // 2
NEXP = E + 2
IH = INTER // 2
EPS_STAT = 1e-6
EPS_NORM = 1e-5
SETS = 4
NPAR = 15


class Line:

    def __init__(self, sems):
        self.sems, self.n = sems, {k: 0 for k in sems}

    def done(self, eng, ins):
        ins.then_inc(self.sems[eng], 1)
        self.n[eng] += 1
        return eng, self.n[eng]

    def after(self, engine, *marks):
        for eng, n in marks:
            engine.wait_ge(self.sems[eng], n)


class Steps:
    LEAD = 4

    def __init__(self, new_sem, per, engine):
        self.per = per
        self.sem = {name: new_sem(name) for name in per}
        for name, s in self.sem.items():
            engine.sem_inc(s, self.LEAD * per[name])


class Turn:

    def __init__(self, steps, clock, stage, i, c, stride):
        self.steps, self.clock, self.stage, self.i, self.c, self.stride = steps, clock, stage, i, c, stride
        self.n, self.waits = {}, []

    def need(self, engine, step, k=None, back=0):
        self.waits.append((engine, step, self.steps.per[step] if k is None else k, self.c - back))

    def emit_waits(self):
        for engine, step, k, c in self.waits:
            per = self.steps.per[step]
            engine.wait_ge(self.steps.sem[step], self.i * (self.stride * per) + (c + self.steps.LEAD) * per + k)
        self.waits = []

    def done(self, step, ins):
        ins.then_inc(self.steps.sem[step], 1)
        self.n[step] = self.n.get(step, 0) + 1
        self.clock.at[step, self.c, self.n[step]] = self.clock.now

    def close(self, steps):
        for s in steps:
            assert self.n.get(s, 0) == self.steps.per[s], (s, self.n.get(s, 0))


class Clock:
    HOP = 0.2

    def __init__(self):
        self.at, self.free, self.now, self.running = {}, {}, 0.0, {}

    def start(self, turn, eng):
        t = self.free.get(eng, 0.0)
        for _, step, k, c in turn.waits:
            if (step, c, k) in self.at:
                t = max(t, self.at[step, c, k] + self.HOP)
            elif c >= self.running.get(step, c + 1):
                return None
        return t

    def run(self, stages, steps_of):
        self.running = {s: turn.c for turn, _ in stages for s in steps_of[turn.stage]}
        for s, c in self.running.items():
            for k in range(1, 16):
                self.at.pop((s, c, k), None)
        live = [[turn, g, next(g)] for turn, g in stages]
        while live:
            best = None
            for n, (turn, g, (eng, step)) in enumerate(live):
                t = self.start(turn, eng)
                if t is not None and (best is None or t < best[0] - 0.05):
                    best = t, n
            assert best, [(x[0].stage, x[2][1], x[0].waits) for x in live]
            t, n = best
            turn, g, (eng, step) = live[n]
            turn.emit_waits()
            self.now = self.free[eng] = t + LENGTH[step]
            live[n][2] = next(g, None)
            if live[n][2] is None:
                assert not turn.waits
                live.pop(n)


PROJ = dict(pcur=1, pq=1, pk=1, pv=1, tap0=3, taps=9, silu=3, vT=1, vtok=1, vhat=1, vh2=1, eb=1, prod=1, e2=1,
            v2=1, ksq=2, kcol=1, red=2, rt=3)
GATE = dict(pg=1, pow=1, cos=5, sT=1, sTs=1, hid=1, hidS=1, z=1, zs=2, sg=1, bexp=1,
            beta=4, bc0=1, bc1=1, bc2=1, kn=1, kb=1, gx=1, dq=1, dqc=1, dqk=1, rl=1, sp=3, lt=3, ss=1, dec=1, kq=2)
TREE = dict(lvl=LEVELS, putm=LEVELS, put=LEVELS, mkq=LEVELS, msuf=LEVELS, mdec=LEVELS, cd=1, kT=1, kTs=1)
INV = dict(tinit=1, tx=LEVELS, txs=LEVELS, ty=LEVELS, ts=LEVELS, tr=LEVELS, trs=LEVELS)
CHAIN = dict(st_p=NC - 1, st_r=NC, st_u=NC, st_us=NC, st_o=NC, st_os=NC, st_k=NC - 1, st_s=NC - 1,
             o2=1, or2=1, of=3, opow=1, of2=1, on=1, oT=1, fin=1)
STEPS = dict(proj=PROJ, gate=GATE, tree=TREE, inverse=INV, chain=CHAIN)
AHEAD = dict(proj=3, gate=2, tree=1, inverse=1, chain=0)
LENGTH = dict(
    pcur=.1, pq=1.7, pk=1.7, pv=1.7, tap0=.57, taps=.66, silu=.52, vT=.22, vtok=.48, vhat=.85, vh2=.48, eb=.6, prod=.6,
    e2=.52, v2=1.23, ksq=1.23, kcol=.25, red=1.4, rt=.07, pg=.85, pow=4.3, cos=.07, sT=.1, sTs=.16, hid=.85, hidS=1.8,
    z=.15, zs=.07, sg=1.9, bexp=.1, beta=.1, bc0=.85, bc1=.85, bc2=.85, kn=.6, kb=.6, gx=.6, dq=1.23, dqc=.1, dqk=.07,
    rl=.4, sp=.52, lt=.9, ss=.6, dec=.62, kq=.6, lvl=.85, putm=.35, put=.35, mkq=.67, msuf=.75, mdec=.5, cd=.07, kT=.22,
    kTs=.48, tinit=2.5, tx=.43, txs=.33, ty=.43, ts=.33, tr=.22, trs=.48, st_p=.21, st_r=.26, st_u=.21, st_us=.16,
    st_k=.21, st_o=.42, st_s=.26, st_os=.27, o2=1.23, or2=.6, of=.07, opow=1., of2=.07, on=1.23, oT=.22, fin=.66)


def program(nc, a, out):
    with ExitStack() as ctx:
        def sb(name, shape, dt=F32):
            return ctx.enter_context(nc.sbuf_tensor(name, shape, dt))

        def sem(name):
            return ctx.enter_context(nc.semaphore(name))

        te, ve, se, ge, sy = nc.tensor, nc.vector, nc.scalar, nc.gpsimd, nc.sync
        bank = [ctx.enter_context(nc.psum_tensor(f"bank{i}", [P, 512], F32)) for i in range(8)]
        line = Line({k: sem("line_" + k) for k in ("te", "ve", "se", "ge")})
        done, after = line.done, line.after
        s_const, s_x, s_w, s_out = sem("s_const"), sem("s_x"), sem("s_w"), sem("s_out")
        s_early = sem("s_early")

        ident = sb("ident", [P, P])
        lmask = sb("lmask", [P, LEVELS, HALF], I32)
        fmask = sb("fmask", [P, LEVELS, HALF])
        xmask = sb("xmask", [P, LEVELS, HALF])
        expo = sb("expo", [P, 6, NC])
        mhalf = sb("mhalf", [P, TB])
        before = sb("before", [P, E, E])
        ones = sb("ones", [P, 1])
        zeros = sb("zeros", [P, 2 * P])
        wsv = sb("wsv", [P, P])
        w1 = sb("w1", [4 * NC, NC, 2 * MLP])
        w2 = sb("w2", [2 * MLP, 2])
        b2 = sb("b2", [P, 2])
        alog = sb("alog", [P, NH])
        pall = sb("pall", [P, NH, NPAR])
        norm_w = sb("norm_w", [P, 1])
        gate_w = sb("gate_w", [P, KB, E])
        wg1 = sb("wg1", [P, KB, P])
        x = sb("x", [P, TB, H])
        xT = sb("xT", [P, KB, TOK])

        n_const = {s_early: 0, s_const: 0}

        def const(dst, src, eng=sy, s=s_const):
            eng.dma_start(dst, src).then_inc(s, 16)
            n_const[s] += 16

        for n in range(0, TB, 2):
            sy.dma_start(x[:, n:n + 2, :], a["x"][n * P:(n + 2) * P].rearrange("(n p) d -> p n d", p=P))\
                .then_inc(s_x, 16)
        const(mhalf[:, :], a["mhalf"], s=s_early)
        const(ident[:, :], a["ident"], s=s_early)
        const(gate_w[:, :, :], a["gate_w"], s=s_early)
        const(before[:, :, :], a["before"], s=s_early)
        m_zero = done("ve", ve.memset(zeros[:, :], 0.0))
        m_ones = done("ve", ve.memset(ones[:, :], 1.0))
        m_w1 = done("ve", ve.memset(w1[:, :, :], 0.0))
        m_w2 = done("ve", ve.memset(w2[:, :], 0.0))
        se.wait_ge(line.sems["ve"], m_w2[1])
        for c in range(NC):
            for m, (w, bias) in enumerate((("Wb1", "bb1"), ("Wa1", "ba1"))):
                const(w1[4 * c:4 * c + 3, c, m * MLP:(m + 1) * MLP], a[w], se)
                const(w1[4 * c + 3:4 * c + 4, c, m * MLP:(m + 1) * MLP], a[bias].rearrange("(o m) -> o m", o=1), se)
        for m, (w, bias) in enumerate((("Wb2", "bb2"), ("Wa2", "ba2"))):
            const(w2[m * MLP:(m + 1) * MLP, m:m + 1], a[w].rearrange("o m -> m o"), se)
            const(b2[:, m:m + 1], a[bias].rearrange("(o m) -> o m", o=1).to_broadcast([P, 1]), se)
        const(wsv[:, :], a["WsvT"])
        const(lmask[:, :, :], a["lmask"])
        const(fmask[:, :, :], a["fmask"])
        const(xmask[:, :, :], a["xmask"])
        const(expo[:, :, :], a["expo"])
        const(alog[:, :], a["A_log"].rearrange("(o m) -> o m", o=1).to_broadcast([P, NH]), se)
        const(pall[:, :, 0:NPAR - 1], a["par"])
        const(norm_w[:, :], a["norm_w"].rearrange("(m o) -> m o", o=1))
        const(wg1[:, :, :], a["Wg1T"])
        for eng in (te, ve, se, ge):
            eng.wait_ge(s_early, n_const[s_early])
            eng.wait_ge(s_x, 16 * TB // 2)

        REG = NH * TOK + 512
        region = sb("region", [P, REG])
        xn = region[:, REG - TB * H:REG].rearrange("p (n d) -> p n d", n=TB)

        stats = sb("stats", [P, TB, 6])
        mv = sb("mv", [P, TB, 2])
        rstd = sb("rstd", [P, TB])

        def layernorm(ready, free):
            after(te, *free)
            copied = []
            for g in range(0, TB, TB // 2):
                if ready:
                    after(ve, *ready[g // 2:(g + TB // 2) // 2])
                layernorm_blocks(range(g, g + TB // 2), copied)
            return [copied[-1]]

        def layernorm_blocks(blocks, copied):
            lo, hi = blocks[0], blocks[-1] + 1
            for n in blocks:
                m = done("ve", ve.bn_stats(stats[:, n, :], x[:, n, :]))
            after(ve, m)
            for n in blocks:
                m = done("ve", ve.bn_aggr(mv[:, n, :], stats[:, n, :]))
            after(ve, m)
            m = done("ve", ve.tensor_scalar(rstd[:, lo:hi], mv[:, lo:hi, 1], EPS_NORM, None, ALU.add))
            after(ge, m)
            m = done("ge", ge.tensor_tensor(rstd[:, lo:hi], rstd[:, lo:hi], mhalf[:, lo:hi], ALU.pow))
            after(ve, m)
            rows = {n: done("ve", ve.tensor_scalar(xn[:, n, :], x[:, n, :], mv[:, n, 0:1], rstd[:, n:n + 1],
                                                   ALU.subtract, ALU.mult)) for n in blocks}
            for n in blocks:
                after(te, rows[n])
                if n >= 2:
                    after(te, copied[n - 2])
                for k in range(KB):
                    t = te.transpose(bank[6 + n % 2][:, k * P:(k + 1) * P], xn[:, n, k * P:(k + 1) * P], ident[:, :])
                t = done("te", t)
                after(se, t)
                copied.append(done("se", se.copy(xT[:, :, n * P:(n + 1) * P],
                                                 bank[6 + n % 2][:, 0:KB * P].rearrange("p (k t) -> p k t", k=KB))))

        score = sb("score", [P, TB, E])
        tmp = sb("tmp", [P, TB, E])
        rowv = sb("rowv", [P, TB])
        comb = sb("comb", [P, TB, NEXP])
        RING = 3
        s_fw = [sem(f"s_fw{r}") for r in range(RING)]

        def ffn(tag, ready, region, free):
            gu = region[:, 0:RING * KB * 2 * INTER].rearrange("p (r k i) -> p r k i", r=RING, k=KB)
            off = RING * KB * 2 * INTER
            wd = region[:, off:off + RING * 2 * H].rearrange("p (r k i) -> p r k i", r=RING, k=2)
            off += RING * 2 * H
            cmp = region[:, off:off + TB * E * E].rearrange("p (t e f) -> p t e f", t=TB, e=E)
            cmp2 = region[:, off + TB * E * E:off + 2 * TB * E * E].rearrange("p (t e f) -> p t e f", t=TB, e=E)
            off += 2 * TB * E * E
            sg = region[:, off:off + 2 * INTER].rearrange("p (r i) -> p r i", r=2)
            off += 2 * INTER
            act = region[:, off:off + 2 * INTER].rearrange("p (r i) -> p r i", r=2)
            off += 2 * INTER
            actT = region[0:IH, off:off + 4 * P].rearrange("p (r k t) -> p r k t", r=2, k=2)
            st = Steps(lambda n: sem(tag + n), dict(gu=TB, sg=TB, act=TB, tr=TB, trs=TB, dn=TB), ge)
            LEAD = st.LEAD * TB

            base = ffn.loaded

            def load(e, slot):
                sy.dma_start(gu[:, slot, :, :], a["w_gu"][bass.ds(e, 1)].rearrange("o p k i -> p (o k) i"))\
                    .then_inc(s_fw[slot], 16)
                sy.dma_start(wd[0:IH, slot, :, :], a["w_dn"][bass.ds(e, 1)].rearrange("o p k i -> p (o k) i"))\
                    .then_inc(s_fw[slot], 16)

            after(sy, *free)
            for r in range(RING):
                load(r, r)

            after(te, *ready)
            for n in range(TB):
                for k in range(KB):
                    t = te.matmul(bank[2][:, n * E:(n + 1) * E], xT[:, k, n * P:(n + 1) * P], gate_w[:, k, :],
                                  start=(k == 0), stop=(k == KB - 1))
            t = done("te", t)
            after(ve, t)

            def step(ins):
                m = done("ve", ins)
                after(ve, m)
                return m

            def wide(v):
                return v[:, :].unsqueeze(2).to_broadcast([P, TB, E])

            lg = bank[2][:, 0:TB * E].rearrange("p (t e) -> p t e", t=TB)
            step(ve.tensor_reduce(rowv[:, :], lg, AX.X, ALU.max))
            m = step(ve.tensor_tensor(tmp[:, :, :], lg, wide(rowv), ALU.subtract))
            after(se, m)
            m = done("se", se.activation(score[:, :, :], tmp[:, :, :], ACT.Exp))
            after(ve, m)
            step(ve.tensor_reduce(rowv[:, :], score[:, :, :], AX.X, ALU.add))
            step(ve.reciprocal(rowv[:, :], rowv[:, :]))
            step(ve.tensor_tensor(score[:, :, :], score[:, :, :], wide(rowv), ALU.mult))
            for n in range(TB):
                mine = score[:, n, :].unsqueeze(2).to_broadcast([P, E, E])
                theirs = score[:, n, :].unsqueeze(1).to_broadcast([P, E, E])
                ve.tensor_tensor(cmp[:, n, :, :], theirs, mine, ALU.is_gt)
                m = done("ve", ve.tensor_tensor(cmp2[:, n, :, :], theirs, mine, ALU.is_equal))
            after(ve, m)
            for n in range(TB):
                m = done("ve", ve.tensor_tensor(cmp2[:, n, :, :], cmp2[:, n, :, :], before[:, :, :], ALU.mult))
            after(ve, m)
            step(ve.tensor_tensor(cmp, cmp, cmp2, ALU.add))
            step(ve.tensor_reduce(tmp[:, :, :], cmp, AX.X, ALU.add))
            step(ve.scalar_tensor_tensor(comb[:, :, 0:E], tmp[:, :, :], float(TOPK), score[:, :, :],
                                         ALU.is_lt, ALU.mult))
            step(ve.tensor_reduce(rowv[:, :], comb[:, :, 0:E], AX.X, ALU.add))
            step(ve.reciprocal(rowv[:, :], rowv[:, :]))
            ve.memset(comb[:, :, E:NEXP], 1.0)
            step(ve.tensor_tensor(comb[:, :, 0:E], comb[:, :, 0:E], wide(rowv), ALU.mult))

            for q in range(4):
                te.matmul(bank[4 + q][:, :], zeros[:, 0:P], xT[:, 0, 0:512], start=True, stop=False,
                          skip_group_check=True)

            def experts(it, last_turn):
                seq = [(r, n) for r in range(RING) for n in range(TB)]

                def cnt(i):
                    return it * (RING * TB) + i + 1 + LEAD

                def wait(eng, s, i):
                    eng.wait_ge(st.sem[s], cnt(i))

                def stage_gu(i):
                    r, n = seq[i]
                    if n == 0:
                        te.wait_ge(s_fw[r], it * 32 + (base + 32))
                    wait(te, "act", i - 2)
                    for k in range(KB):
                        t = te.matmul(bank[i % 2][:, 0:2 * INTER], xT[:, k, n * P:(n + 1) * P], gu[:, r, k, :],
                                      start=(k == 0), stop=(k == KB - 1))
                    t.then_inc(st.sem["gu"], 1)
                    wait(se, "gu", i)
                    wait(se, "act", i - 2)
                    se.activation(sg[:, i % 2, :], bank[i % 2][:, 0:INTER], ACT.Silu).then_inc(st.sem["sg"], 1)
                    wait(ve, "sg", i)
                    wait(ve, "tr", i - 2)
                    ve.scalar_tensor_tensor(act[:, i % 2, :], bank[i % 2][:, INTER:2 * INTER],
                                            comb[:, n, bass.ds(it * RING + r, 1)], sg[:, i % 2, :],
                                            ALU.mult, ALU.mult).then_inc(st.sem["act"], 1)

                def stage_tr(i):
                    wait(te, "act", i)
                    wait(te, "trs", i - 2)
                    for k in range(2):
                        t = te.transpose(bank[2 + i % 2][0:IH, k * P:(k + 1) * P], act[:, i % 2, k * IH:(k + 1) * IH],
                                         ident[:, :])
                    t.then_inc(st.sem["tr"], 1)
                    wait(se, "tr", i)
                    wait(se, "dn", i - 2)
                    se.copy(actT[:, i % 2, :, :], bank[2 + i % 2][0:IH, 0:2 * P].rearrange("p (k t) -> p k t", k=2))\
                        .then_inc(st.sem["trs"], 1)

                def stage_dn(i):
                    r, n = seq[i]
                    wait(te, "trs", i)
                    for k in range(2):
                        t = te.matmul(bank[4 + n // 2][:, (n % 2) * H:(n % 2 + 1) * H], actT[:, i % 2, k, :],
                                      wd[0:IH, r, k, :], start=False, stop=False, skip_group_check=True)
                    t.then_inc(st.sem["dn"], 1)

                last = len(seq)
                for i in range(last + 2):
                    if i < last:
                        stage_gu(i)
                    if 1 <= i <= last:
                        stage_tr(i - 1)
                    if i >= 2:
                        stage_dn(i - 2)
                        r, n = seq[i - 2]
                        if n == TB - 1:
                            if not last_turn:
                                sy.wait_ge(st.sem["dn"], cnt(i - 2))
                                load(it * RING + (r + RING), r)

            turns = NEXP // RING
            with nc.Fori(0, turns - 1) as it:
                experts(it, False)
            experts(turns - 1, True)
            ffn.loaded = base + NEXP // RING * 32

            ve.wait_ge(st.sem["dn"], NEXP * TB + LEAD)
            marks = []
            for q in range(4):
                marks.append(done("ve", ve.scalar_tensor_tensor(
                    x[:, 2 * q:2 * q + 2, :].rearrange("p a d -> p (a d)"), bank[4 + q][:, :], 0.5,
                    x[:, 2 * q:2 * q + 2, :].rearrange("p a d -> p (a d)"), ALU.mult, ALU.add)))
            return marks

        ffn.loaded = 0

        m_x = layernorm([], [])
        m_ffn = ffn("f1_", m_x, region, [])
        for eng in (te, ve, se, ge):
            eng.wait_ge(s_const, n_const[s_const])
        m = done("se", se.activation(alog[:, :], alog[:, :], ACT.Exp))
        after(ve, m)
        m_par = done("ve", ve.tensor_scalar(pall[:, :, NPAR - 1], alog[:, :], -1.0, None, ALU.mult))
        m_ln = layernorm(m_ffn, [m_ffn[-1]])
        m_att, m_wo = attention(nc, ctx, sb, sem, a, line, bank, dict(
            ident=ident, lmask=lmask, fmask=fmask, xmask=xmask, expo=expo, ones=ones, wsv=wsv, w1=w1, w2=w2, b2=b2, pall=pall,
            norm_w=norm_w, wg1=wg1, zeros=zeros, xT=xT, x=x, s_w=s_w,
            o_all=region[:, 0:NH * TOK].rearrange("p (h t) -> p h t", h=NH)), m_ln + [m_par])
        after(ve, m_wo)
        m_ln = layernorm(m_att, [])
        m_fin = ffn("f2_", m_ln, region, [m_wo])
        for q in range(4):
            after(sy, m_fin[q])
            sy.dma_start(out[2 * q * P:2 * (q + 1) * P].rearrange("(n p) d -> p n d", p=P),
                         x[:, 2 * q:2 * q + 2, :]).then_inc(s_out, 16)
        sy.wait_ge(s_out, 16 * 4)


def attention(nc, ctx, sb, sem, a, line, bank, cs, ready):
    te, ve, se, ge, sy = nc.tensor, nc.vector, nc.scalar, nc.gpsimd, nc.sync
    done, after = line.done, line.after
    ident, xT, s_w = cs["ident"], cs["xT"], cs["s_w"]
    F = bank[0:2]
    G = bank[2]
    L = bank[3:5]
    I = bank[5]
    S = bank[6:8]

    wqkv = sb("wqkv", [P, 3, KB, P])
    wg2 = sb("wg2", [P, P])
    g1 = sb("g1", [P, TOK])

    pcur = sb("pcur", [P, 2, NPAR])
    cv = [sb(f"conv_{n}", [P, 2, T]) for n in "qk"] + [sb("conv_v", [P, 1, T])]
    sq = sb("sq", [P, 4, NC * P])
    eb = sb("eb", [P, NC * P])
    ksq = sb("ksq", [P, 2, T])
    red = sb("red", [P, 2, 4, NC])
    rts = sb("rts", [P, 2, 6, NC])
    rt = sb("rt", [P, 6, NC])
    cosb = sb("cosb", [P, 2, NC])
    s_in = sb("s_in", [P, 2, NC, 4])
    sTs = sb("sTs", [4 * NC, P])
    hid = sb("hid", [2 * MLP, T])
    z = sb("z", [P, NC, 2])
    bz = sb("bz", [P, NC])
    tokf = sb("tokf", [P, 2, NC])
    gx = sb("gx", [P, T])
    dq = gx
    yv = sb("yv", [P, T])
    lnv = sb("lnv", [P, T])
    t1 = sb("t1", [P, T])
    vtok = sb("vtok", [P, SETS, NC, P])
    beta = sb("beta", [P, SETS, NC])
    rq = sb("rq", [P, SETS, NC])
    dqk = sb("dqk", [P, SETS, NC])
    KQ = sb("KQ", [P, SETS, 2, T])
    suf = sb("suf", [P, 2, T])
    dec = sb("dec", [P, 2, 2 * T])
    AT = sb("AT", [P, 2, NC, P])
    Mb = sb("Mb", [P, 2, NC, P])
    TT = sb("TT", [P, 2, NC, P])
    kT = sb("kT", [P, 2, NC, P])
    cd = sb("cd", [P, 2, NC])
    Tm = sb("Tm", [P, NC, P])
    X = sb("X", [P, NC, HALF])
    R = sb("R", [P, 2, P])
    U = sb("U", [P, 2, P])
    St = sb("St", [P, 2, P])
    ot = sb("ot", [P, NC, P])
    o2 = sb("o2", [P, NC, P])
    of = sb("of", [P, 4, NC])
    nhalf = cs["expo"][:, 3, :]

    s_g = sem("s_g")
    clock = Clock()
    st = Steps(sem, {s: n for stage in STEPS.values() for s, n in stage.items()}, ge)
    scale = float(DK) ** -0.5

    def load_head(h):
        sy.dma_start(wqkv[:, :, :, :], a["wqkv"][h]).then_inc(s_w, 16)

    def load_gate(h):
        sy.dma_start(wg2[:, :], a["Wg2T"][h]).then_inc(s_g, 16)

    load_head(0)
    load_gate(0)
    ve.memset(AT[:, :, :, :], 0.0)
    ve.memset(Mb[:, :, :, :], 0.0)
    m0 = done("ve", ve.memset(s_in[:, :, :, :], 1.0))
    after(ve, m0)
    after(te, *ready)
    after(ve, *ready)
    for n in range(TOK // 512):
        for k in range(KB):
            t = te.matmul(bank[3 + n][:, :], cs["wg1"][:, k, :], xT[:, k, n * 512:(n + 1) * 512],
                          start=(k == 0), stop=(k == KB - 1))
        t = done("te", t)
        after(se, t)
        m3 = done("se", se.copy(g1[:, n * 512:(n + 1) * 512], bank[3 + n][:, :]))
    after(te, m3)

    def proj(t, i, c):
        need, fin = t.need, t.done
        h, b, q4 = i * (SETS // B) + c // B, c % B, c % SETS
        w = pcur[:, b, :]
        conv = [cv[0][:, b, :], cv[1][:, b, :], cv[2][:, 0, :]]
        qS, kS, vS = conv
        tok = slice(b * T, (b + 1) * T)

        need(ve, "dec", back=2)
        need(ve, "sg", back=2)
        yield ve, "pcur"
        fin("pcur", ve.tensor_scalar(w, cs["pall"][:, bass.ds(h, 1), :].rearrange("p o n -> p (o n)"), 1.0, None,
                                     ALU.mult))
        last = 0
        for p, (j, name, bk) in enumerate(((1, "pk", 0), (2, "pv", 1), (0, "pq", 0))):
            if p == 0:
                need(te, "prod", back=1)
                need(te, "eb", back=1)
                need(te, "vh2", back=1)
            elif p == 1:
                need(te, "rt", back=1)
                need(te, "vtok", back=1)
            else:
                need(te, "taps", 3)
                need(te, "tap0", 1)
            yield te, name
            if p == 0:
                te.wait_ge(s_w, h * 16 + 16)
            for k in range(KB):
                m = te.matmul(F[bk][:, :], wqkv[:, j, k, :], xT[:, k, tok], start=(k == 0), stop=(k == KB - 1))
            fin(name, m)
            need(se, name)
            need(se, "pcur")
            if j == 0:
                need(se, "dq", back=2)
                need(se, "kq", back=2)
                need(se, "ksq", 2, back=2)
            elif j == 1:
                need(se, "ksq", 1, back=2)
                need(se, "vhat", back=2)
                need(se, "kb", back=2)
                need(se, "kn", back=2)
                need(se, "gx", back=2)
            else:
                need(se, "vT", back=1)
            yield se, "tap0"
            fin("tap0", se.activation(conv[j], F[bk][:, :], ACT.Copy, scale=w[:, 4 * j + 3:4 * j + 4]))
            for d in range(1, CONV):
                need(ve, "pcur")
                if d == 1:
                    need(ve, "tap0", p + 1)
                else:
                    need(ve, "taps", 3 * p + d - 1)
                yield ve, "taps"
                fin("taps", ve.scalar_tensor_tensor(conv[j][:, d:T], F[bk][:, 0:T - d],
                                                    w[:, 4 * j + 3 - d:4 * j + 4 - d], conv[j][:, d:T],
                                                    ALU.mult, ALU.add))
            need(se, "taps", 3 * p + 3)
            yield se, "silu"
            fin("silu", se.activation(conv[j], conv[j], ACT.Silu))
            if j == 1:
                need(ge, "silu", 1)
                need(ge, "kcol", back=1)
                yield ge, "ksq"
                fin("ksq", ge.tensor_tensor(ksq[:, 0, :], kS, kS, ALU.mult))
            elif j == 2:
                need(te, "silu", 2)
                yield te, "vT"
                for n in range(NC):
                    m = te.transpose(F[1][:, n * P:(n + 1) * P], vS[:, n * P:(n + 1) * P], ident[:, :])
                fin("vT", m)
        vt = vtok[:, q4, :, :].rearrange("p n v -> p (n v)")
        need(se, "vT")
        need(se, "st_r", back=SETS)
        yield se, "vtok"
        fin("vtok", se.copy(vt, F[1][:, :]))
        need(te, "taps", 9)
        need(te, "silu", 1)
        yield te, "vhat"
        for n in range(NC):
            m = te.matmul(F[0][:, n * P:(n + 1) * P], kS[:, n * P:(n + 1) * P], cs["wsv"][:, :], start=True, stop=True)
        fin("vhat", m)
        need(se, "vhat")
        need(se, "red", back=1)
        yield se, "vh2"
        fin("vh2", se.activation(sq[:, 1, :], F[0][:, :], ACT.Square))
        need(ge, "silu", 3)
        need(ge, "kcol", back=1)
        yield ge, "ksq"
        fin("ksq", ge.tensor_tensor(ksq[:, 1, :], qS, qS, ALU.mult))
        need(ve, "vtok")
        need(ve, "vh2")
        need(ve, "e2", back=1)
        yield ve, "eb"
        fin("eb", ve.tensor_tensor(eb[:, :], F[0][:, :], vt, ALU.subtract))
        yield ve, "prod"
        fin("prod", ve.tensor_tensor(sq[:, 3, :], F[0][:, :], vt, ALU.mult))
        need(ge, "vtok")
        need(ge, "red", back=1)
        yield ge, "v2"
        fin("v2", ge.tensor_tensor(sq[:, 2, :], vt, vt, ALU.mult))
        need(se, "eb")
        yield se, "e2"
        fin("e2", se.activation(sq[:, 0, :], eb[:, :], ACT.Square))
        need(te, "ksq")
        need(te, "vtok")
        yield te, "kcol"
        for j in range(2):
            for n in range(NC):
                m = te.matmul(F[1][:, 4 * j + n:4 * j + n + 1], ksq[:, j, n * P:(n + 1) * P], cs["ones"][:, :],
                              start=True, stop=True)
        fin("kcol", m)
        need(ve, "eb")
        need(ve, "sT", back=2)
        yield ve, "red"
        fin("red", ve.tensor_reduce(s_in[:, b, :, 1], eb[:, :].rearrange("p (n v) -> p n v", n=NC), AX.X, ALU.add,
                                    apply_absolute_value=True))
        need(ve, "cos", 4, back=2)
        for s in ("prod", "vh2", "v2", "e2"):
            need(ve, s)
        yield ve, "red"
        fin("red", ve.tensor_reduce(red[:, b, :, :].rearrange("p a n -> p (a n)"),
                                    sq[:, :, :].rearrange("p a (n v) -> p (a n) v", n=NC), AX.X, ALU.add))
        need(ve, "red")
        need(ve, "pow", back=2)
        yield ve, "rt"
        fin("rt", ve.tensor_scalar(rts[:, b, 0:3, :], red[:, b, 0:3, :], EPS_STAT, None, ALU.add))
        need(ve, "kcol")
        yield ve, "rt"
        fin("rt", ve.tensor_scalar(rts[:, b, 3:5, :].rearrange("p a n -> p (a n)"), F[1][:, 0:2 * NC], EPS_STAT, None,
                                   ALU.add))
        yield ve, "rt"
        fin("rt", ve.tensor_scalar(rts[:, b, 5, :], F[1][:, 0:NC], 1e-24, None, ALU.max))
        t.close(PROJ)

    def gate(t, i, c):
        need, fin = t.need, t.done
        h, b, q4 = i * (SETS // B) + c // B, c % B, c % SETS
        w = pcur[:, b, :]
        qS, kS = cv[0][:, b, :], cv[1][:, b, :]
        tok = slice(b * T, (b + 1) * T)
        need(te, "dqk", back=1)
        need(te, "kb", back=1)
        yield te, "pg"
        te.wait_ge(s_g, h * 16 + 16)
        fin("pg", te.matmul(G[:, :], wg2[:, :], g1[:, tok], start=True, stop=True))
        need(se, "pg")
        need(se, "pcur")
        yield se, "sg"
        fin("sg", se.activation(cs["o_all"][:, bass.ds(h, 1), tok].rearrange("p o t -> p (o t)"), G[:, :],
                                ACT.Sigmoid, bias=w[:, 13:14]))
        need(ge, "rt")
        need(ge, "bc0", back=1)
        need(ge, "beta", back=1)
        yield ge, "pow"
        fin("pow", ge.tensor_tensor(rt[:, :, :], rts[:, b, :, :], cs["expo"][:, :, :], ALU.pow))
        need(ve, "pow")
        yield ve, "cos"
        fin("cos", ve.tensor_tensor(cosb[:, 0, :], rt[:, 1, :], rt[:, 2, :], ALU.mult))
        need(ve, "cos", 1)
        yield ve, "cos"
        fin("cos", ve.tensor_scalar(cosb[:, 0, :], cosb[:, 0, :], EPS_STAT, None, ALU.add))
        need(ve, "cos", 2)
        yield ve, "cos"
        fin("cos", ve.reciprocal(cosb[:, 1, :], cosb[:, 0, :]))
        need(ve, "cos", 3)
        yield ve, "cos"
        fin("cos", ve.scalar_tensor_tensor(cosb[:, 0, :], red[:, b, 3, :], -1.0, cosb[:, 1, :], ALU.mult, ALU.mult))
        ve.tensor_copy(s_in[:, b, :, 0], rt[:, 0, :])
        need(ve, "cos", 4)
        yield ve, "cos"
        fin("cos", ve.tensor_scalar(s_in[:, b, :, 2], cosb[:, 0, :], 1.0, None, ALU.add))
        need(te, "cos")
        need(te, "sg")
        yield te, "sT"
        fin("sT", te.transpose(G[0:4 * NC, 0:P], s_in[:, b, :, :].rearrange("p n j -> p (n j)"), ident[:, :]))
        need(se, "sT")
        need(se, "hid", back=1)
        yield se, "sTs"
        fin("sTs", se.copy(sTs[:, :], G[0:4 * NC, 0:P]))
        need(te, "sTs")
        yield te, "hid"
        for n in range(NC):
            m = te.matmul(G[0:2 * MLP, n * P:(n + 1) * P], cs["w1"][:, n, :], sTs[:, :], start=True, stop=True)
        fin("hid", m)
        need(se, "z", back=1)
        need(se, "hid")
        yield se, "hidS"
        fin("hidS", se.activation(hid[:, :], G[0:2 * MLP, :], ACT.Silu))
        se.preload_act_table_set("natural_log_exp_and_others")
        need(te, "hidS")
        yield te, "z"
        for n in range(NC):
            m = te.matmul(G[:, 2 * n:2 * n + 2], hid[:, n * P:(n + 1) * P], cs["w2"][:, :],
                          start=True, stop=True)
        fin("z", m)
        need(ve, "z")
        yield ve, "zs"
        fin("zs", ve.tensor_tensor(z[:, :, :], G[:, 0:2 * NC].rearrange("p (n j) -> p n j", n=NC),
                                   cs["b2"][:, :].unsqueeze(1).to_broadcast([P, NC, 2]), ALU.add))
        need(ve, "zs", 1)
        yield ve, "zs"
        fin("zs", ve.tensor_scalar(bz[:, :], z[:, :, 0], -87.0, None, ALU.max))
        need(se, "zs")
        yield se, "bexp"
        fin("bexp", se.activation(bz[:, :], bz[:, :], ACT.Exp, scale=-1.0))
        need(ve, "bexp")
        yield ve, "beta"
        fin("beta", ve.tensor_scalar(bz[:, :], bz[:, :], 1.0, None, ALU.add))
        need(ve, "of2", back=SETS)
        ve.tensor_scalar(rq[:, q4, :], rt[:, 4, :], scale, None, ALU.mult)
        need(ve, "bc1", back=1)
        need(ve, "st_r", back=SETS)
        need(ve, "zs")
        yield ve, "beta"
        fin("beta", ve.tensor_tensor(tokf[:, 1, :], rt[:, 5, :], z[:, :, 1], ALU.mult))
        need(ve, "beta", 1)
        yield ve, "beta"
        fin("beta", ve.reciprocal(beta[:, q4, :], bz[:, :]))
        need(ve, "beta", 3)
        yield ve, "beta"
        fin("beta", ve.tensor_tensor(tokf[:, 0, :], rt[:, 3, :], beta[:, q4, :], ALU.mult))
        def along(src):
            for n in range(NC):
                m = te.matmul(G[:, n * P:(n + 1) * P], src[:, n:n + 1].to_broadcast([P, P]), ident[:, :],
                              start=True, stop=True)
            return m

        need(te, "beta", 2)
        need(te, "zs", 1)
        yield te, "bc2"
        fin("bc2", along(tokf[:, 1, :]))
        need(ve, "bc2")
        need(ve, "lt", back=1)
        need(ve, "sp", back=1)
        need(ve, "dqc", back=1)
        yield ve, "gx"
        fin("gx", ve.tensor_tensor(gx[:, :], kS, G[:, :], ALU.mult))
        need(se, "gx")
        need(se, "lt", back=1)
        yield se, "sp"
        fin("sp", se.activation(yv[:, :], gx[:, :], ACT.Abs, bias=w[:, 12:13]))
        need(se, "sp", 1)
        yield se, "sp"
        fin("sp", se.activation(yv[:, :], yv[:, :], ACT.Exp, scale=-1.0))
        need(te, "gx")
        yield te, "bc0"
        fin("bc0", along(rt[:, 3, :]))
        need(ve, "bc0")
        need(ve, "kT", back=2)
        yield ve, "kn"
        fin("kn", ve.tensor_tensor(suf[:, b, :], kS, G[:, :], ALU.mult))
        need(te, "kn")
        need(te, "beta")
        yield te, "bc1"
        fin("bc1", along(tokf[:, 0, :]))
        need(ve, "bc1")
        need(ve, "st_o", back=SETS)
        yield ve, "kb"
        fin("kb", ve.tensor_tensor(KQ[:, q4, 0, :], kS, G[:, :], ALU.mult))
        need(ve, "sp", 1)
        yield ve, "rl"
        fin("rl", ve.tensor_scalar(gx[:, :], gx[:, :], w[:, 12:13], 0.0, ALU.add, ALU.max))
        need(se, "sp", 2)
        need(se, "ss", back=1)
        yield se, "sp"
        fin("sp", se.activation(lnv[:, :], yv[:, :], ACT.Ln, bias=1.0))
        need(ve, "sp", 2)
        yield ve, "lt"
        fin("lt", ve.tensor_scalar(t1[:, :], yv[:, :], 1.0, 1.0, ALU.add, ALU.subtract))
        need(ge, "lt", 1)
        yield ge, "lt"
        fin("lt", ge.tensor_tensor(t1[:, :], yv[:, :], t1[:, :], ALU.subtract))
        need(ge, "rl")
        need(ge, "lt", 2)
        yield ge, "lt"
        fin("lt", ge.tensor_tensor(t1[:, :], t1[:, :], gx[:, :], ALU.add))
        need(ge, "kn")
        need(ge, "lt", 3)
        yield ge, "dq"
        fin("dq", ge.tensor_tensor(dq[:, :], suf[:, b, :], qS, ALU.mult))
        need(te, "dq")
        need(te, "kb")
        yield te, "dqc"
        for n in range(NC):
            m = te.matmul(G[:, n:n + 1], dq[:, n * P:(n + 1) * P], cs["ones"][:, :], start=True, stop=True)
        fin("dqc", m)
        need(ve, "sp", 3)
        need(ve, "lt", 3)
        yield ve, "ss"
        fin("ss", ve.tensor_tensor(lnv[:, :], lnv[:, :], t1[:, :], ALU.add))
        need(se, "ss")
        need(se, "msuf", back=2)
        need(se, "mkq", back=2)
        need(se, "cd", back=2)
        yield se, "dec"
        fin("dec", se.activation(dec[:, b, 0:T], lnv[:, :], ACT.Exp, scale=w[:, 14:15]))
        need(ve, "dqc")
        need(ve, "st_os", back=SETS)
        yield ve, "dqk"
        fin("dqk", ve.tensor_copy(dqk[:, q4, :], G[:, 0:NC]))
        need(ve, "dec")
        need(ve, "kb")
        yield ve, "kq"
        fin("kq", ve.tensor_tensor(KQ[:, q4, 0, :], KQ[:, q4, 0, :], dec[:, b, 0:T], ALU.mult))
        yield ve, "kq"
        fin("kq", ve.tensor_tensor(KQ[:, q4, 1, :], qS, dec[:, b, 0:T], ALU.mult))
        t.close(GATE)

    def tree(t, i, c):
        need, fin = t.need, t.done
        b, q4 = c % B, c % SETS
        kq, sf = KQ[:, q4, :, :], suf[:, b, :]
        src, off = 0, T
        for l in range(LEVELS):
            s = 1 << l
            nb = HALF // s
            if l == 0:
                need(te, "kq")
                need(te, "kn")
                need(te, "kTs", back=1)
                need(te, "put", back=1)
                need(te, "putm", back=1)
            else:
                need(te, "mkq", l)
                need(te, "msuf", l)
                if l >= 2:
                    need(te, "put", l - 1)
                    need(te, "putm", l - 1)
            yield te, "lvl"
            for n in range(NC):
                right = kq[:, :, n * P:(n + 1) * P].rearrange("p q (m two r) -> p q m two r", two=2, r=s)[:, :, :, 1, :]
                dst = L[l % 2][:, n * P:(n + 1) * P].rearrange("p (q m r) -> p q m r", q=2, r=s)
                m = te.matmul(dst, sf[:, n * P:(n + 1) * P], right, start=True, stop=True)
            fin("lvl", m)
            M = NC * nb
            d = dec[:, b, src:src + 2 * M].rearrange("p (m two) -> p m two", two=2)
            need(ve, "lvl", l + 1)
            if l:
                need(ve, "mdec", l)
                need(ve, "mkq", l)
                need(ve, "put", l)
            else:
                need(ve, "st_o", back=2)
            yield ve, "mkq"
            kr = kq.rearrange("p q (m two r) -> p q m two r", two=2, r=s)[:, :, :, 1, :]
            dl = d[:, :, 0:1].rearrange("p m o -> p (m o)").unsqueeze(2).to_broadcast([P, M, s])
            for q in range(2):
                i = ve.tensor_tensor(kr[:, q, :, :], kr[:, q, :, :], dl, ALU.mult)
            fin("mkq", i)
            sleft = sf.rearrange("p (m two r) -> p m two r", two=2, r=s)[:, :, 0, :]
            need(ge, "lvl", l + 1)
            need(ge, "dq")
            if l:
                need(ge, "mdec", l)
                need(ge, "msuf", l)
            else:
                need(ge, "dec")
            yield ge, "mdec"
            fin("mdec", ge.tensor_tensor(dec[:, b, off:off + M], d[:, :, 0], d[:, :, 1], ALU.mult))
            yield ge, "msuf"
            fin("msuf", ge.tensor_tensor(sleft, sleft, d[:, :, 1].unsqueeze(2).to_broadcast([P, M, s]), ALU.mult))
            src, off = off, off + M
            both = L[l % 2][:, :].rearrange("p (n q m r) -> p n q m r", n=NC, q=2, r=s)
            need(ve, "tx", *((l - 1,) if l >= 2 else (LEVELS - l, 1)))
            yield ve, "putm"
            fin("putm", ve.tensor_tensor(
                Mb[:, l % 2, :, :].rearrange("p n (m two r) -> p n m two r", two=2, r=s)[:, :, :, 1, :],
                both[:, :, 0, :, :],
                cs["fmask"][:, l, :].rearrange("p (m r) -> p m r", r=s).unsqueeze(1).to_broadcast([P, NC, nb, s]),
                ALU.mult))
            yield ve, "put"
            fin("put", ve.copy_predicated(
                AT[:, b, :, :].rearrange("p n (m two r) -> p n m two r", two=2, r=s)[:, :, :, 1, :],
                cs["lmask"][:, l, :].rearrange("p (m r) -> p m r", r=s).unsqueeze(1).to_broadcast([P, NC, nb, s]),
                both[:, :, 1, :, :]))
        need(ve, "mdec")
        need(ve, "st_s", back=2)
        yield ve, "cd"
        fin("cd", ve.tensor_copy(cd[:, b, :], dec[:, b, src:src + NC]))
        need(te, "msuf")
        need(te, "put")
        need(te, "putm")
        yield te, "kT"
        for n in range(NC):
            m = te.transpose(L[0][:, n * P:(n + 1) * P], sf[:, n * P:(n + 1) * P], ident[:, :])
        fin("kT", m)
        need(se, "kT")
        need(se, "st_k", back=2)
        yield se, "kTs"
        fin("kTs", se.copy(kT[:, b, :, :].rearrange("p n v -> p (n v)"), L[0][:, :]))
        t.close(TREE)

    def inverse(t, i, c):
        need, fin = t.need, t.done
        b = c % B
        TT_ = TT[:, b, :, :]
        idb = ident[:, :].unsqueeze(1).to_broadcast([P, NC, P])
        zb = cs["zeros"][:, 0:P].unsqueeze(1).to_broadcast([P, NC, P])
        need(ge, "st_u", back=2)
        need(ge, "tr", back=1)
        yield ge, "tinit"
        ge.tensor_tensor(Tm[:, :, :], idb, zb, ALU.add)
        fin("tinit", ge.tensor_tensor(TT_, idb, zb, ALU.add))
        for l in range(LEVELS):
            s = 1 << l
            left = Tm[:, :, :].rearrange("p n (m two r) -> p n m two r", two=2, r=s)[:, :, :, 0, :]
            need(te, "putm", l + 1)
            if l == 0:
                need(te, "tinit")
                need(te, "trs", back=1)
            else:
                need(te, "ts", l)
                need(te, "trs", l)
            yield te, "tx"
            x0 = I[:, 0:NC * HALF].rearrange("p (n m r) -> p n m r", n=NC, r=s)
            for n in range(NC):
                m = te.matmul(x0[:, n, :, :], Mb[:, l % 2, n, :], left[:, n, :, :], start=True, stop=True)
            fin("tx", m)
            need(ve, "tx", l + 1)
            if l:
                need(ve, "ty", l)
            else:
                need(ve, "ty", back=1)
            yield ve, "txs"
            fin("txs", ve.tensor_tensor(X[:, :, :], I[:, 0:NC * HALF].rearrange("p (n m) -> p n m", n=NC),
                                        cs["xmask"][:, l, :].unsqueeze(1).to_broadcast([P, NC, HALF]), ALU.mult))
            need(te, "txs", l + 1)
            if l:
                need(te, "trs", l)
            yield te, "ty"
            for n in range(NC):
                m = te.matmul(I[:, n * HALF:(n + 1) * HALF], TT_[:, n, :], X[:, n, :], start=True, stop=True)
            fin("ty", m)
            need(ve, "ty", l + 1)
            if l:
                need(ve, "tr", l)
                need(ve, "ts", l)
            else:
                need(ve, "tinit")
            yield ve, "ts"
            fin("ts", ve.tensor_tensor(left, left, I[:, 0:NC * HALF].rearrange("p (n m r) -> p n m r", n=NC, r=s),
                                       ALU.add))
            need(te, "ts", l + 1)
            yield te, "tr"
            for n in range(NC):
                m = te.transpose(I[:, n * P:(n + 1) * P], Tm[:, n, :], ident[:, :])
            fin("tr", m)
            need(se, "tr", l + 1)
            need(se, "tinit")
            yield se, "trs"
            fin("trs", se.copy(TT_.rearrange("p n v -> p (n v)"), I[:, :]))
        t.close(INV)

    def chain(t, i, c):
        need, fin = t.need, t.done
        h, b, q4 = i * (SETS // B) + c // B, c % B, c % SETS
        kq, v_, beta_ = KQ[:, q4, :, :], vtok[:, q4, :, :], beta[:, q4, :]
        for n in range(NC):
            r = n % 2
            if n == 0:
                need(ve, "vtok")
                need(ve, "st_u", back=1)
                yield ve, "st_r"
                fin("st_r", ve.tensor_scalar(R[:, r, :], v_[:, n, :], beta_[:, n:n + 1], None, ALU.mult))
            else:
                need(te, "st_s", n)
                yield te, "st_p"
                fin("st_p", te.matmul(S[0][:, 0:P], kq[:, 0, n * P:(n + 1) * P], St[:, r, :], start=True, stop=True))
                need(ve, "st_p", n)
                yield ve, "st_r"
                fin("st_r", ve.scalar_tensor_tensor(R[:, r, :], v_[:, n, :], beta_[:, n:n + 1], S[0][:, 0:P],
                                                    ALU.mult, ALU.subtract))
            need(te, "st_r", n + 1)
            if n == 0:
                need(te, "trs")
                need(te, "st_os", back=1)
            else:
                need(te, "st_os", n)
            yield te, "st_u"
            fin("st_u", te.matmul(S[1][:, 0:P], TT[:, b, n, :], R[:, r, :], start=True, stop=True))
            need(se, "st_u", n + 1)
            if n == 0:
                need(se, "st_os", back=1)
            elif n >= 2:
                need(se, "st_os", n - 1)
            yield se, "st_us"
            fin("st_us", se.copy(U[:, r, :], S[1][:, 0:P]))
            need(te, "st_us", n + 1)
            if n < NC - 1:
                if n == 0:
                    need(te, "kTs")
                    need(te, "fin", back=1)
                yield te, "st_k"
                fin("st_k", te.matmul(S[0][:, 0:P], kT[:, b, n, :], U[:, r, :], start=True, stop=True))
            yield te, "st_o"
            if n:
                te.matmul(S[1][:, 0:P], kq[:, 1, n * P:(n + 1) * P], St[:, r, :], start=True, stop=False)
            fin("st_o", te.matmul(S[1][:, 0:P], AT[:, b, n, :], U[:, r, :], start=(n == 0), stop=True))
            if n < NC - 1:
                need(ve, "st_k", n + 1)
                if n == 0:
                    need(ve, "st_o", back=1)
                    yield ve, "st_s"
                    fin("st_s", ve.tensor_copy(St[:, 1 - r, :], S[0][:, 0:P]))
                else:
                    need(ve, "st_o", n)
                    need(ve, "st_s", n)
                    need(ve, "cd")
                    yield ve, "st_s"
                    fin("st_s", ve.scalar_tensor_tensor(St[:, 1 - r, :], St[:, r, :], cd[:, b, n:n + 1],
                                                        S[0][:, 0:P], ALU.mult, ALU.add))
            need(ve, "st_o", n + 1)
            if n == 0:
                need(ve, "on", back=1)
                need(ve, "o2", back=1)
            yield ve, "st_os"
            fin("st_os", ve.scalar_tensor_tensor(ot[:, n, :], U[:, r, :], dqk[:, q4, n:n + 1], S[1][:, 0:P],
                                                 ALU.mult, ALU.add))
        need(ge, "st_os")
        need(ge, "or2", back=1)
        yield ge, "o2"
        fin("o2", ge.tensor_tensor(o2[:, :, :], ot[:, :, :], ot[:, :, :], ALU.mult))
        need(ve, "o2")
        need(ve, "opow", back=1)
        yield ve, "or2"
        fin("or2", ve.tensor_reduce(of[:, 0, :], o2[:, :, :], AX.X, ALU.add))
        yield ve, "of"
        fin("of", ve.tensor_tensor(of[:, 1, :], rq[:, q4, :], rq[:, q4, :], ALU.mult))
        need(ve, "or2")
        need(ve, "of", 1)
        yield ve, "of"
        fin("of", ve.tensor_tensor(of[:, 0, :], of[:, 0, :], of[:, 1, :], ALU.mult))
        need(ve, "of", 2)
        yield ve, "of"
        fin("of", ve.tensor_scalar(of[:, 0, :], of[:, 0, :], 1.0 / DK, EPS_NORM, ALU.mult, ALU.add))
        need(ge, "of")
        yield ge, "opow"
        fin("opow", ge.tensor_tensor(of[:, 2, :], of[:, 0, :], nhalf, ALU.pow))
        need(ve, "opow")
        need(ve, "on", back=1)
        yield ve, "of2"
        fin("of2", ve.tensor_tensor(of[:, 3, :], of[:, 2, :], rq[:, q4, :], ALU.mult))
        need(ge, "of2")
        need(ge, "oT", back=1)
        yield ge, "on"
        fin("on", ge.tensor_tensor(o2[:, :, :], ot[:, :, :], of[:, 3, :].unsqueeze(2).to_broadcast([P, NC, P]),
                                   ALU.mult))
        need(te, "on")
        need(te, "st_s")
        yield te, "oT"
        for n in range(NC):
            m = te.transpose(S[0][:, n * P:(n + 1) * P], o2[:, n, :], ident[:, :])
        fin("oT", m)
        place = cs["o_all"][:, bass.ds(h, 1), b * T:(b + 1) * T].rearrange("p o t -> p (o t)")
        need(ve, "sg")
        need(ve, "oT")
        yield ve, "fin"
        fin("fin", ve.scalar_tensor_tensor(place, S[0][:, :], cs["norm_w"][:, 0:1], place, ALU.mult, ALU.mult))
        t.close(CHAIN)

    def stages(i, j, units=NH * B):
        live = []
        for f in (inverse, tree, chain, gate, proj):
            c = j + AHEAD[f.__name__]
            if not isinstance(i, int) or 0 <= i * SETS + c < units:
                t = Turn(st, clock, f.__name__, i, c, SETS)
                live.append((t, f(t, i, c)))
        clock.run(live, STEPS)
        for stage, step, load in (("proj", "pq", load_head), ("gate", "pg", load_gate)):
            c = j + AHEAD[stage]
            if c % B == B - 1 and (not isinstance(i, int) or 0 < i * SETS + c < units - 1):
                t = Turn(st, clock, stage, i, c, SETS)
                t.need(sy, step)
                t.emit_waits()
                load(i * (SETS // B) + c // B + 1)

    turns = NH * B // SETS
    for j in range(-max(AHEAD.values()), 0):
        stages(0, j)
    with nc.Fori(0, turns - 1) as i:
        for j in range(SETS):
            stages(i, j)
    for j in range(SETS):
        stages(turns - 1, j)

    units = NH * B + st.LEAD
    wo = [sq[:, :, :].rearrange("p q t -> p (q t)").rearrange("p (h d) -> p h d", d=H),
          KQ[:, 0:2, :, :].rearrange("p b q t -> p (b q t)").rearrange("p (h d) -> p h d", d=H)]
    sy.wait_ge(st.sem["red"], units * PROJ["red"])
    sy.dma_start(wo[0], a["WoT"][:, 0:NH // 2, :]).then_inc(s_w, 16)
    sy.wait_ge(st.sem["st_o"], (units - 2) * CHAIN["st_o"])
    sy.dma_start(wo[1], a["WoT"][:, NH // 2:NH, :]).then_inc(s_w, 16)
    te.wait_ge(s_w, NH * 16 + 32)
    te.wait_ge(st.sem["fin"], units)
    te.wait_ge(st.sem["dqk"], units)
    marks = []
    for n in range(TB):
        for h in range(NH):
            m = te.matmul(bank[n // 2][:, (n % 2) * H:(n % 2 + 1) * H], cs["o_all"][:, h, n * P:(n + 1) * P],
                          wo[h // (NH // 2)][:, h % (NH // 2), :], start=(h == 0), stop=(h == NH - 1))
        if n % 2:
            m = done("te", m)
            after(ve, m)
            rows = cs["x"][:, n - 1:n + 1, :].rearrange("p a d -> p (a d)")
            marks.append(done("ve", ve.tensor_tensor(rows, rows, bank[n // 2][:, :], ALU.add)))
    return marks, m


def constants():
    p, l, m = np.arange(P)[:, None, None], np.arange(LEVELS)[None, :, None], np.arange(HALF)[None, None, :]
    s = 1 << l
    child, block = p // s, m // s
    expo = np.full((P, 6, NC), -0.5, np.float32)
    expo[:, 0:3] = 0.5
    return dict(ident=np.eye(P, dtype=np.float32), lmask=(child == 2 * block).astype(np.int32), fmask=(child == 2 * block).astype(np.float32),
                xmask=-(child == 2 * block + 1).astype(np.float32), expo=expo,
                mhalf=np.full((P, TB), -0.5, np.float32),
                before=np.broadcast_to(np.tri(E, E, -1, dtype=np.float32), (P, E, E)))


def layout(v):
    g = {k.split("_", 2)[2]: np.asarray(x) for k, x in v.items() if k.startswith("L0_attn")}
    f = {k.split("_", 2)[2]: np.asarray(x) for k, x in v.items() if k.startswith("L0_ffn")}
    heads = [g[k].reshape(NH, P, KB, P).transpose(0, 3, 2, 1) for k in ("Wq", "Wk", "Wv")]
    par = [g[k].reshape(NH, P, CONV) for k in ("conv_q", "conv_k", "conv_v")]
    par += [g[k].reshape(NH, P, 1) for k in ("dt_bias", "bg2")]
    rows = dict(x=g["hidden_states"].reshape(TOK, H), wqkv=np.stack(heads, 2),
                Wg2T=g["Wg2"].reshape(NH, P, P).transpose(0, 2, 1),
                par=np.concatenate(par, 2).transpose(1, 0, 2),
                Wg1T=g["Wg1"].reshape(P, KB, P).transpose(2, 1, 0), WsvT=g["Wsv"].T,
                WoT=g["Wo"].reshape(H, NH, P).transpose(2, 1, 0), A_log=g["A_log"], norm_w=g["norm_w"],
                Wb1=g["Wb1"].T, Wa1=g["Wa1"].T, gate_w=f["gate_w"].reshape(E, KB, P).transpose(2, 1, 0))
    rows.update({k: g[k] for k in ("bb1", "ba1", "Wb2", "Wa2", "bb2", "ba2")})

    def up(w):
        return w.reshape(-1, KB, P, INTER).transpose(0, 2, 1, 3)

    def shared(w):
        return w.reshape(H, 2, INTER).transpose(1, 0, 2)

    gate = np.concatenate([up(f["w_gate"]), up(shared(f["sw_gate"]))], 0)
    upw = np.concatenate([up(f["w_up"]), up(shared(f["sw_up"]))], 0)
    rows["w_gu"] = np.concatenate([gate, upw], 3)
    dn = np.concatenate([f["w_down"], f["sw_down"].reshape(2, INTER, H)], 0)
    rows["w_dn"] = dn.reshape(NEXP, 2, IH, H).transpose(0, 2, 1, 3)
    rows.update(constants())
    return {k: np.ascontiguousarray(w) for k, w in rows.items()}


def kernel(**inputs):
    import concourse.bacc as bacc
    from concourse.bass_utils import run_bass_kernel_spmd as run

    nc = bacc.Bacc("TRN2", target_bir_lowering=False, num_devices=1)
    arrays = layout(inputs)
    aps = {k: nc.dram_tensor("in_" + k, w.shape, mybir.dt.from_np(w.dtype), kind="ExternalInput").ap()
           for k, w in arrays.items()}
    out = nc.dram_tensor("out", (TOK, H), F32, kind="ExternalOutput").ap()
    program(nc, aps, out)
    r = run(nc, [{"in_" + k: w for k, w in arrays.items()}], core_ids=[0])
    return r.results[0]["out"].reshape(B, T, H)
```
